# Optimizing a Trainium2 kernel written in Bass

```python
import numpy as np
import jax
import jax.numpy as jnp

def _softmax(x, axis=-1):
    return jax.nn.softmax(x, axis=axis)

def _gelu(x):
    return jax.nn.gelu(x, approximate=True)

def _silu(x):
    return jax.nn.silu(x)

def _sigmoid(x):
    return jax.nn.sigmoid(x)

def _layernorm(x, axis=-1, eps=1e-05):
    m = jnp.mean(x, axis=axis, keepdims=True)
    v = jnp.var(x, axis=axis, keepdims=True)
    return (x - m) / jnp.sqrt(v + eps)

def _scatter_add(tgt, idx, src, axis=0):
    return tgt.at[idx].add(src)

def _segment_sum(src, seg, n):
    return jax.ops.segment_sum(src, seg, n)
kernel_name = 'mk_flamingo_gated_d1_seqx_r4_a5a2f7'

def setup_inputs(seed: int=0):
    np.random.seed(seed)
    _w = jnp.asarray

    def _rec_inputs():
        import jax
        import jax.numpy as jnp
        _rk = jax.random.key(seed)
        x = -0.0002928 + 1 * jax.random.normal(jax.random.fold_in(_rk, 1), (16, 256, 256), jnp.float32)
        _lenS = 256 - jax.random.randint(jax.random.fold_in(_rk, 7), (16,), 0, max(1, 256 // 4) + 1, jnp.int32)
        _lenS2 = 256 - jax.random.randint(jax.random.fold_in(_rk, 8), (16,), 0, max(1, 256 // 4) + 1, jnp.int32)
        _ctx_1024P = jax.random.normal(jax.random.fold_in(_rk, 11), (16, 16, 256), jnp.float32)
        _ctx_1024c = jax.random.dirichlet(jax.random.fold_in(_rk, 511), 0.3 * jnp.ones((16,), jnp.float32), (16, 256))
        _ctx_1024t = jnp.einsum('bsk,bkd->bsd', _ctx_1024c, _ctx_1024P)
        _ctx_1024t = _ctx_1024t * jax.lax.rsqrt(jnp.mean(jnp.square(_ctx_1024t)) + 1e-12) * 0.953939
        ctx_1024 = -1.39393e-06 + 0.999914 * (_ctx_1024t + 0.3 * jax.random.normal(jax.random.fold_in(_rk, 611), (16, 256, 256), jnp.float32))
        _g = jax.random.normal(jax.random.fold_in(_rk, 9001), (2, 1), jnp.float32)
        _g = jnp.sign(_g) * jnp.maximum(jnp.abs(_g), 1.0) + (_g == 0) * 1.0
        g_xattn = _g[0]
        g_ffn = _g[1]
        return (x, ctx_1024, g_xattn, g_ffn)
    x, ctx_1024, g_xattn, g_ffn = _rec_inputs()

    def _L0_xattn_setup():
        import jax, jax.numpy as jnp
        import numpy as np
        B, S, H, NH = (2, 512, 256, 4)
        DH = H // NH
        EPS = 1e-06

        def _parallel_stabilized(qh, kh, vh, ig, fg):
            log_fg = jax.nn.log_sigmoid(fg)
            cs = jnp.cumsum(log_fg, axis=2)
            ltr = jnp.tril(jnp.ones((qh.shape[2], qh.shape[2]), dtype=bool))
            log_fg_mat = jnp.where(ltr, cs - jnp.swapaxes(cs, 2, 3), -jnp.inf)
            log_D = log_fg_mat + jnp.swapaxes(ig, 2, 3)
            max_log_D = jnp.max(log_D, axis=-1, keepdims=True)
            D = jnp.exp(log_D - max_log_D)
            qk = jnp.einsum('bhsd,bhtd->bhst', qh, kh) / jnp.sqrt(jnp.float32(DH))
            C = qk * D
            normalizer = jnp.maximum(jnp.abs(jnp.sum(C, axis=-1, keepdims=True)), jnp.exp(-max_log_D))
            return jnp.einsum('bhst,bhtd->bhsd', C / (normalizer + EPS), vh)
        key = jax.random.key(seed)
        ks = jax.random.split(key, 6)
        q = jax.random.normal(ks[0], (B, S, H), dtype=jnp.float32)
        k = jax.random.normal(ks[1], (B, S, H), dtype=jnp.float32)
        v = jax.random.normal(ks[2], (B, S, H), dtype=jnp.float32)
        igate_kernel = jax.random.normal(ks[3], (3 * H, NH), dtype=jnp.float32) * 0.02
        fgate_kernel = jax.random.normal(ks[4], (3 * H, NH), dtype=jnp.float32) * 0.02
        igate_bias = jax.random.normal(ks[5], (NH,), dtype=jnp.float32) * 0.1
        fgate_bias = jnp.linspace(3.0, 6.0, NH, dtype=jnp.float32)
        outnorm_scale = jnp.ones((H,), dtype=jnp.float32)
        return {'q': q, 'k': k, 'v': v, 'igate_kernel': igate_kernel, 'igate_bias': igate_bias, 'fgate_kernel': fgate_kernel, 'fgate_bias': fgate_bias, 'outnorm_scale': outnorm_scale}
    _L0_xattn_all = _L0_xattn_setup()
    _L0_xattn_in = {k: v for k, v in _L0_xattn_all.items() if k in ('igate_kernel', 'igate_bias', 'fgate_kernel', 'fgate_bias', 'outnorm_scale')}
    del _L0_xattn_all

    def _L0_ffn_setup():
        import jax, jax.numpy as jnp
        import numpy as np
        key = jax.random.key(seed)
        kx, kw = jax.random.split(key)
        x = jax.random.normal(kx, (32, 1024, 256), dtype=jnp.float32)
        weight = jax.random.normal(kw, (256, 256), dtype=jnp.float32) * 0.01
        return {'x': x, 'weight': weight}
    _L0_ffn_all = _L0_ffn_setup()
    _L0_ffn_in = {k: v for k, v in _L0_ffn_all.items() if k in ('weight',)}
    del _L0_ffn_all
    return {'x': x, 'ctx_1024': ctx_1024, 'g_xattn': g_xattn, 'g_ffn': g_ffn, 'L0_xattn_igate_kernel': _L0_xattn_in['igate_kernel'], 'L0_xattn_igate_bias': _L0_xattn_in['igate_bias'], 'L0_xattn_fgate_kernel': _L0_xattn_in['fgate_kernel'], 'L0_xattn_fgate_bias': _L0_xattn_in['fgate_bias'], 'L0_xattn_outnorm_scale': _L0_xattn_in['outnorm_scale'], 'L0_ffn_weight': _L0_ffn_in['weight']}

def reference(x, ctx_1024, g_xattn, g_ffn, L0_xattn_igate_kernel, L0_xattn_igate_bias, L0_xattn_fgate_kernel, L0_xattn_fgate_bias, L0_xattn_outnorm_scale, L0_ffn_weight):
    import jax
    import jax.numpy as jnp

    def _L0_xattn_ref(q, k, v, igate_kernel, igate_bias, fgate_kernel, fgate_bias, outnorm_scale):
        import jax, jax.numpy as jnp
        import numpy as np
        B, S, H, NH = (2, 512, 256, 4)
        DH = H // NH
        EPS = 1e-06

        def _parallel_stabilized(qh, kh, vh, ig, fg):
            log_fg = jax.nn.log_sigmoid(fg)
            cs = jnp.cumsum(log_fg, axis=2)
            ltr = jnp.tril(jnp.ones((qh.shape[2], qh.shape[2]), dtype=bool))
            log_fg_mat = jnp.where(ltr, cs - jnp.swapaxes(cs, 2, 3), -jnp.inf)
            log_D = log_fg_mat + jnp.swapaxes(ig, 2, 3)
            max_log_D = jnp.max(log_D, axis=-1, keepdims=True)
            D = jnp.exp(log_D - max_log_D)
            qk = jnp.einsum('bhsd,bhtd->bhst', qh, kh) / jnp.sqrt(jnp.float32(DH))
            C = qk * D
            normalizer = jnp.maximum(jnp.abs(jnp.sum(C, axis=-1, keepdims=True)), jnp.exp(-max_log_D))
            return jnp.einsum('bhst,bhtd->bhsd', C / (normalizer + EPS), vh)
        Bq, Sq, Hq = q.shape
        x = jnp.concatenate([q, k, v], axis=-1)
        ig = x @ igate_kernel + igate_bias
        fg = x @ fgate_kernel + fgate_bias
        ig = jnp.transpose(ig, (0, 2, 1))[..., None]
        fg = jnp.transpose(fg, (0, 2, 1))[..., None]
        qh = jnp.transpose(q.reshape(Bq, Sq, NH, DH), (0, 2, 1, 3))
        kh = jnp.transpose(k.reshape(Bq, Sq, NH, DH), (0, 2, 1, 3))
        vh = jnp.transpose(v.reshape(Bq, Sq, NH, DH), (0, 2, 1, 3))
        h = _parallel_stabilized(qh, kh, vh, ig, fg)
        mean = jnp.mean(h, axis=-1, keepdims=True)
        var = jnp.mean((h - mean) ** 2, axis=-1, keepdims=True)
        h_norm = (h - mean) * jax.lax.rsqrt(var + 1e-05)
        h_norm = h_norm * outnorm_scale.reshape(1, NH, 1, DH)
        out = jnp.transpose(h_norm, (0, 2, 1, 3)).reshape(Bq, Sq, Hq)
        return out

    def _L0_ffn_ref(x, weight):
        import jax, jax.numpy as jnp
        import numpy as np
        b_weight = jnp.sign(weight)
        return jnp.einsum('bsi,oi->bso', x, b_weight)
    x = x + jnp.tanh(g_xattn[0]) * _L0_xattn_ref(_layernorm(x, axis=-1), ctx_1024, ctx_1024, L0_xattn_igate_kernel, L0_xattn_igate_bias, L0_xattn_fgate_kernel, L0_xattn_fgate_bias, L0_xattn_outnorm_scale)
    x = x + jnp.tanh(g_ffn[0]) * _L0_ffn_ref(_layernorm(x, axis=-1), L0_ffn_weight)
    return x

_drawn_inputs = setup_inputs


def setup_inputs(seed=0):
    import zlib

    import numpy as np

    out = dict(_drawn_inputs(seed))
    spreads = {'L0_xattn_outnorm_scale': (1.0, 0.2)}
    factors = {}
    for name, (base, spread) in spreads.items():
        noise = np.random.default_rng([zlib.crc32(name.encode()), seed]).standard_normal(out[name].shape)
        drawn = base * np.exp(spread * noise) if base else spread * noise
        out[name] = jnp.asarray(drawn.astype(out[name].dtype))
    for name, factor in factors.items():
        out[name] = (out[name] * factor).astype(out[name].dtype)
    return out
```

```python
import math
from contextlib import ExitStack

import concourse.bass as bass
from concourse import mybir


def build(nc, x, ctx, g_xattn, g_ffn, igate_kernel, igate_bias, fgate_kernel, fgate_bias,
          outnorm_scale, ffn_weight, out):
    fp32 = mybir.dt.float32
    ALU = mybir.AluOpType
    ACT = mybir.ActivationFunctionType
    AX = mybir.AxisListType

    P = 128
    B, S, H = x.shape
    NH = igate_bias.shape[0]
    DH = H // NH
    NBLK = S // P
    NCH = H // P
    ROWS = B * NH
    VW = DH + 1
    NG = 3 * NH
    LN_EPS = 1e-5
    EPS = 1e-6
    SCALE = math.sqrt(DH)
    SLOTS1 = 4
    DW = S + P

    x_v = x.rearrange("b (k p) d -> b p k d", p=P)
    ctx_v = ctx.rearrange("b (k p) d -> b p k d", p=P)
    out_v = out.rearrange("b (k p) d -> b p k d", p=P)

    es = ExitStack()
    with es:
        def sb(name, shape, dt=fp32):
            return es.enter_context(nc.sbuf_tensor(name, shape, dt))

        def pb(name, shape):
            return es.enter_context(nc.psum_tensor(name, shape, fp32))

        def sem(name):
            return es.enter_context(nc.semaphore(name))

        X = sb("X", [P, B, NBLK, H])
        V1 = sb("V1", [P, B, NBLK, NH, VW])
        QKT = sb("QKT", [P, B, 2, NCH, S])
        qkt = [sb(f"qkt{u}", [P, 2, NCH, S]) for u in range(SLOTS1)]
        ctx_in = sb("ctx_in", [P, SLOTS1, NBLK, H])
        xn = [sb(f"xn{u}", [P, NBLK, H])[:] for u in range(2)]
        ident = sb("ident", [P, P])
        wi = sb("wi", [P, 3 * NCH, NH])
        wf = sb("wf", [P, 3 * NCH, NH])
        wg = sb("wg", [P, 2 * NCH, NG])
        gbias = sb("gbias", [P, 2 * NH])
        gates_in = sb("gates_in", [P, 2])
        tanh_g = sb("tanh_g", [P, 2])
        scale_in = sb("scale_in", [P, H])
        scale_g = sb("scale_g", [P, H])
        w_in = sb("w_in", [P, NCH, H])
        w_pos = sb("w_pos", [P, NCH, H])
        w_neg = sb("w_neg", [P, NCH, H])
        sgnT = sb("sgnT", [P, NCH, H])
        stats = [sb(f"stats{u}", [P, NBLK, 6]) for u in range(2)]
        mv = [sb(f"mv{u}", [P, NBLK, 2]) for u in range(2)]
        veps = [sb(f"veps{u}", [P, NBLK]) for u in range(2)]
        rstd = [sb(f"rstd{u}", [P, NBLK]) for u in range(2)]
        half_neg = sb("half_neg", [P, NBLK * NH])
        G = sb("G", [P, B, NBLK, NG])
        gi = sb("gi", [P, NBLK, ROWS])
        gf = sb("gf", [P, NBLK, ROWS])
        gabs = sb("gabs", [P, NBLK, ROWS])
        gexp = sb("gexp", [P, NBLK, ROWS])
        gln = sb("gln", [P, NBLK, ROWS])
        logf = sb("logf", [P, NBLK, ROWS])
        zeros = sb("zeros", [ROWS, S])
        cs = sb("cs", [ROWS, S])
        a_row = sb("a_row", [ROWS, S])
        m_row = sb("m_row", [ROWS, S])
        maxd_row = sb("maxd_row", [ROWS, S])
        a_col = sb("a_col", [P, NBLK, ROWS])
        floor_col = sb("floor_col", [P, NBLK, ROWS])
        m_all = [qkt[2 + u][:].rearrange("p w c s -> p (w c) s") for u in range(2)]
        D = [sb(f"D{u}", [P, NH, DW]) for u in range(2)]
        C = [sb(f"C{u}", [P, NH, DW]) for u in range(2)]
        sq, hn, hsc = (ctx_in[:, i].rearrange("p k (h d) -> p (k h) d", d=DH) for i in range(3))
        x2T = ctx_in[:, 3]
        ssq = sb("ssq", [P, NBLK * NH])[:]
        nrm_a = sb("nrm_a", [P, NBLK * NH])
        nrm_b = sb("nrm_b", [P, NBLK * NH])
        nrm_c = sb("nrm_c", [P, NBLK * NH])
        nrm_d = sb("nrm_d", [P, NBLK * NH])
        var_n = sb("var_n", [P, NBLK * NH])
        zed = sb("zed", [P, NBLK * NH])
        hrs = sb("hrs", [P, NBLK * NH])
        m_dram = nc.dram_tensor("m_scratch", [ROWS, S], fp32, kind="Internal").ap()

        bank_n = [pb(f"bank_n{u}", [P, NBLK, 512]) for u in range(2)]
        bank_a = [pb(f"bank_a{u}", [P, 512]) for u in range(2)]
        bank_x = pb("bank_x", [P, 512])[:]
        bank_f = pb("bank_f", [P, 512])[:]
        ps_q = [bank_n[u][:, 0, :] for u in range(2)]
        ps_c = [bank_n[u][:, 1, :] for u in range(2)]
        ps_g = [bank_a[u][:, 0:NBLK * NG].rearrange("p (k g) -> p k g", k=NBLK) for u in range(2)]
        ps_irow = bank_x[0:ROWS, 0:S]
        ps_frow = bank_f[0:ROWS, 0:S]
        ps_cols = bank_n[0][:, 0, 0:2 * NBLK * ROWS].rearrange("p (w k r) -> p w k r", w=2, k=NBLK)
        ps_w = bank_n[1][:, 0, :]
        ps_num = [bank_n[u][:, :, 0:NH * VW].rearrange("p k (h v) -> p k h v", h=NH) for u in range(2)]
        ps_qk = bank_a
        ps_x = bank_x
        ps_f = bank_f

        consts_in = sem("consts_in")
        x_in = [sem(f"x_in{u}") for u in range(SLOTS1)]
        c_in = [sem(f"c_in{u}") for u in range(SLOTS1)]
        ident_zeroed, ident_ready, ones_ready, half_ready = sem("ident_zeroed"), sem("ident_ready"), sem("ones_ready"), sem("half_ready")
        zeros_ready = sem("zeros_ready")
        wg_mean0, wg_ready = sem("wg_mean0"), sem("wg_ready")
        tanh_done, scale_done = sem("tanh_done"), sem("scale_done")
        stats_done, mv_done, veps_done, rstd_done, xn_done = sem("stats_done"), sem("mv_done"), sem("veps_done"), sem("rstd_done"), sem("xn_done")
        qT_done, cT_done, qT_copied, cT_copied = sem("qT_done"), sem("cT_done"), sem("qT_copied"), sem("cT_copied")
        gates_done, gates_copied, v_done = sem("gates_done"), sem("gates_copied"), sem("v_done")
        qkt_saved = [sem(f"qkt_saved{u}") for u in range(SLOTS1)]
        w_split, w_sign, w_turned, w_copied = sem("w_split"), sem("w_sign"), sem("w_turned"), sem("w_copied")
        gi_done, gf_done, gabs_done, gexp_done, gln_done, logf_done = (sem("gi_done"), sem("gf_done"), sem("gabs_done"),
                                                                     sem("gexp_done"), sem("gln_done"), sem("logf_done"))
        irow_done, frow_done, cs_done, a_done, m_done, maxd_done = (sem("irow_done"), sem("frow_done"), sem("cs_done"),
                                                                  sem("a_done"), sem("m_done"), sem("maxd_done"))
        cols_done, cols_copied, m_saved = sem("cols_done"), sem("cols_copied"), sem("m_saved")
        qkt_in = [sem(f"qkt_in{u}") for u in range(2)]
        m_in = [sem(f"m_in{u}") for u in range(2)]
        d_done, mask_done, qk_done, c_done, num_done = sem("d_done"), sem("mask_done"), sem("qk_done"), sem("c_done"), sem("num_done")
        sq_done, ssq_done, na_done, nb_done, nc_done, nd_done = (sem("sq_done"), sem("ssq_done"), sem("na_done"),
                                                               sem("nb_done"), sem("nc_done"), sem("nd_done"))
        varn_done, zed_done, hrs_done, hn_done, hsc_done, x2_done = (sem("varn_done"), sem("zed_done"), sem("hrs_done"),
                                                                   sem("hn_done"), sem("hsc_done"), sem("x2_done"))
        stats2_done, mv2_done, veps2_done, rstd2_done, xn2_done = (sem("stats2_done"), sem("mv2_done"), sem("veps2_done"),
                                                                 sem("rstd2_done"), sem("xn2_done"))
        x2T_done, x2T_copied, ffn_done, out_done = sem("x2T_done"), sem("x2T_copied"), sem("ffn_done"), sem("out_done")
        stored = sem("stored")
        held = {e: sem(f"held_{e}") for e in ("SP", "Pool", "DVE")}
        N_CONST_LOADS = 8

        def need(eng, s, count):
            if not (isinstance(count, int) and count <= 0):
                eng.wait_ge(s, count)

        def hold(eng, s, count):
            if isinstance(count, int):
                need(eng, s, count)
            else:
                eng.wait_ge(s, count).then_inc(held[eng.engine.name], 1)

        block = es.enter_context(nc.Block())

        LAST2 = B + 3

        @block.sync
        def _(sp):
            def load_x(n, u, turn):
                if turn is not None:
                    hold(sp, x_in[u], 16 * turn)
                sp.dma_start(X[:, n], x_v[n]).then_inc(x_in[u], 16)

            def load_ctx(n, u, turn):
                if turn is not None:
                    hold(sp, c_in[u], 16 * turn)
                    hold(sp, v_done, n - 3)
                sp.dma_start(ctx_in[:, u], ctx_v[n]).then_inc(c_in[u], 16)

            def save_qkt(n, u):
                hold(sp, qT_copied, n + 1)
                hold(sp, cT_copied, n + 1)
                sp.dma_start(QKT[:, n], qkt[u][:]).then_inc(qkt_saved[u], 16)

            load_x(0, 0, None)
            sp.dma_start(wi[:], igate_kernel.rearrange("(c p) h -> p c h", p=P)).then_inc(consts_in, 16)
            sp.dma_start(wf[:], fgate_kernel.rearrange("(c p) h -> p c h", p=P)).then_inc(consts_in, 16)
            load_ctx(0, 0, None)
            sp.dma_start(gates_in[:, 0:1], g_xattn.partition_broadcast(P)).then_inc(consts_in, 16)
            sp.dma_start(gates_in[:, 1:2], g_ffn.partition_broadcast(P)).then_inc(consts_in, 16)
            load_x(1, 1, None)
            load_ctx(1, 1, None)
            sp.dma_start(scale_in[:], outnorm_scale.partition_broadcast(P)).then_inc(consts_in, 16)
            sp.dma_start(gbias[:, 0:NH], igate_bias.partition_broadcast(P)).then_inc(consts_in, 16)
            sp.dma_start(gbias[:, NH:2 * NH], fgate_bias.partition_broadcast(P)).then_inc(consts_in, 16)
            for n in range(2, SLOTS1):
                load_x(n, n, None)
                load_ctx(n, n, None)
            sp.dma_start(w_in[:], ffn_weight.rearrange("(c p) i -> p c i", p=P)).then_inc(consts_in, 16)
            with sp.Fori(1, B // SLOTS1) as turn:
                for u in range(SLOTS1):
                    load_x(SLOTS1 * turn + u, u, turn)
                    save_qkt(SLOTS1 * (turn - 1) + u, u)
                    load_ctx(SLOTS1 * turn + u, u, turn)
            for u in range(SLOTS1):
                save_qkt(B - SLOTS1 + u, u)

            sp.wait_ge(m_done, 1)
            sp.dma_start(m_dram, m_row[:]).then_inc(m_saved, 16)
            sp.wait_ge(m_saved, 16)
            for u in range(SLOTS1):
                sp.wait_ge(qkt_saved[u], 16 * (B // 4))
            sp.wait_ge(gates_done, B)

            def load2(n, u, turn):
                hold(sp, qk_done, 4 * (n - 1))
                hold(sp, d_done, 4 * (n - 1))
                if not (isinstance(turn, int) and turn == 0):
                    hold(sp, qkt_in[u], 16 * turn)
                    hold(sp, m_in[u], 16 * turn)
                sp.dma_start(m_all[u], m_dram[bass.ds(NH * n, NH), :].rearrange("h s -> (h s)").partition_broadcast(P)
                             ).then_inc(m_in[u], 16)
                sp.dma_start(qkt[u][:], QKT[:, n]).then_inc(qkt_in[u], 16)

            def store(n):
                hold(sp, out_done, n + 1)
                sp.dma_start(out_v[n], X[:, n]).then_inc(stored, 16)

            for n in range(4):
                load2(n, n % 2, n // 2)
            with sp.Fori(0, (B - 4) // 2) as turn:
                for u in range(2):
                    load2(2 * turn + 4 + u, u, turn + 2)
                    store(2 * turn + u)
            for n in range(B - 4, B):
                store(n)
            sp.wait_ge(stored, 16 * B)

        @block.gpsimd
        def _(pool):
            nc.gpsimd.memset(ident[:], 0.0).then_inc(ident_zeroed, 1)
            nc.gpsimd.memset(half_neg[:], -0.5).then_inc(half_ready, 1)
            nc.gpsimd.memset(V1[:, :, :, :, DH:VW].rearrange("p b k h o -> p (b k h) o"), 1.0).then_inc(ones_ready, 1)
            nc.gpsimd.memset(zeros[:], 0.0).then_inc(zeros_ready, 1)
            pool.wait_ge(ident_zeroed, 1)
            nc.gpsimd.affine_select(out=ident[:], in_=ident[:], compare_op=ALU.not_equal, fill=1.0, base=0,
                                    pattern=[[-1, P]], channel_multiplier=1).then_inc(ident_ready, 1)
            pool.wait_ge(half_ready, 1)

            def rsqrt1(n, u):
                pool.wait_ge(mv_done, 2 * n + 2)
                hold(pool, rstd_done, n - 1)
                nc.gpsimd.tensor_scalar(veps[u % 2][:], mv[u % 2][:, :, 1], LN_EPS, None, ALU.add).then_inc(veps_done, 1)
                pool.wait_ge(veps_done, n + 1)
                need(pool, xn_done, 2 * (n - 1))
                nc.gpsimd.tensor_tensor(rstd[u % 2][:], veps[u % 2][:], half_neg[:, 0:NBLK], ALU.pow).then_inc(rstd_done, 1)

            def centre_v(n, u):
                pool.wait_ge(gates_copied, n + 1)
                mean = G[:, n, :, 2 * NH:NG]
                last = None
                for k in range(NBLK):
                    last = nc.gpsimd.tensor_tensor(
                        V1[:, n, k, :, 0:DH],
                        ctx_in[:, u, k, :].rearrange("p (h d) -> p h d", h=NH),
                        mean[:, k, :].unsqueeze(2).to_broadcast([P, NH, DH]), ALU.add)
                last.then_inc(v_done, 1)

            for n in range(SLOTS1):
                rsqrt1(n, n)
                if n >= 2:
                    centre_v(n - 2, n - 2)
            with pool.Fori(1, B // SLOTS1) as turn:
                for u in range(SLOTS1):
                    rsqrt1(SLOTS1 * turn + u, u)
                    centre_v(SLOTS1 * turn + u - 2, (u - 2) % SLOTS1)
            for n in range(B - 2, B):
                centre_v(n, n % SLOTS1)

            def mask(n, u):
                for h in range(NH):
                    hold(pool, d_done, 4 * n + h + 1)
                    diag = D[u][:, h, :].rearrange("p (c s) -> p c s", s=P)[:, 0:3:2, :]
                    nc.gpsimd.affine_select(out=diag, in_=diag, compare_op=ALU.is_ge, fill=0.0, base=0,
                                            pattern=[[0, 2], [1, P]], channel_multiplier=-1).then_inc(mask_done, 1)

            def head_rsqrt(n):
                pool.wait_ge(nb_done, n + 1)
                hold(pool, nd_done, n)
                nc.gpsimd.tensor_scalar(nrm_c[:], nrm_b[:], SCALE * EPS, math.sqrt(LN_EPS), ALU.add, ALU.mult
                                        ).then_inc(nc_done, 1)
                pool.wait_ge(ssq_done, n + 1)
                hold(pool, zed_done, n)
                nc.gpsimd.tensor_scalar(var_n[:], ssq, 1.0 / DH, None, ALU.mult).then_inc(varn_done, 1)
                pool.wait_ge(nc_done, n + 1)
                nc.gpsimd.tensor_tensor(nrm_d[:], nrm_c[:], nrm_c[:], ALU.mult).then_inc(nd_done, 1)
                pool.wait_ge(varn_done, n + 1)
                pool.wait_ge(nd_done, n + 1)
                need(pool, hrs_done, n)
                nc.gpsimd.tensor_tensor(zed[:], var_n[:], nrm_d[:], ALU.add).then_inc(zed_done, 1)
                pool.wait_ge(zed_done, n + 1)
                need(pool, hn_done, n)
                nc.gpsimd.tensor_tensor(hrs[:], zed[:], half_neg[:], ALU.pow).then_inc(hrs_done, 1)

            def residual(n):
                pool.wait_ge(hn_done, n + 1)
                need(pool, x2_done, n)
                nc.gpsimd.tensor_tensor(hsc.rearrange("p (k h) d -> p k (h d)", k=NBLK),
                                        hn.rearrange("p (k h) d -> p k (h d)", k=NBLK),
                                        scale_g[:].unsqueeze(1).to_broadcast([P, NBLK, H]), ALU.mult).then_inc(hsc_done, 1)
                pool.wait_ge(hsc_done, n + 1)
                nc.gpsimd.tensor_tensor(X[:, n], hsc.rearrange("p (k h) d -> p k (h d)", k=NBLK), X[:, n], ALU.add
                                        ).then_inc(x2_done, 1)

            def rsqrt2(n, u):
                pool.wait_ge(mv2_done, 2 * n + 2)
                hold(pool, rstd2_done, n - 1)
                nc.gpsimd.tensor_scalar(veps[u][:], mv[u][:, :, 1], LN_EPS, None, ALU.add).then_inc(veps2_done, 1)
                pool.wait_ge(veps2_done, n + 1)
                need(pool, xn2_done, 2 * (n - 1))
                nc.gpsimd.tensor_tensor(rstd[u][:], veps[u][:], half_neg[:, 0:NBLK], ALU.pow).then_inc(rstd2_done, 1)

            def step(n, u, first, last):
                if first <= 0 <= last:
                    pass
                if 1 in range(first, last + 1):
                    head_rsqrt(n - 1)
                if 2 in range(first, last + 1):
                    rsqrt2(n - 2, u)
                if 1 in range(first, last + 1):
                    residual(n - 1)
                if -1 in range(first, last + 1):
                    mask(n + 1, 1 - u)

            pool.wait_ge(scale_done, 1)
            mask(0, 0)
            for n in range(0, 5):
                step(n, n % 2, -1, min(n, 3))
            with pool.Fori(2, (B - 2) // 2) as turn:
                for v in range(2):
                    step(2 * turn + 1 + v, (1 + v) % 2, -1, 3)
            for n in range(B - 1, LAST2):
                step(n, n % 2, n - B + 1, 3)

        @block.vector
        def _(dve):
            def ln_stats(xrow, u, done_stats, done_mv, n, stats_freed, mv_freed):
                need(dve, stats_freed[0], stats_freed[1])
                for k in range(NBLK):
                    nc.vector.bn_stats(stats[u][:, k, :], xrow[:, k, :]).then_inc(done_stats, 1)
                need(dve, mv_freed[0], mv_freed[1])
                for k in range(NBLK):
                    hold(dve, done_stats, 2 * n + 1 + k)
                    nc.vector.bn_aggr(mv[u][:, k, :], stats[u][:, k, :]).then_inc(done_mv, 1)

            def stats1(n, u):
                ln_stats(X[:, n], u % 2, stats_done, mv_done, n, (mv_done, 2 * (n - 1)), (xn_done, 2 * (n - 1)))

            def norm1(n, u):
                dve.wait_ge(rstd_done, n + 1)
                need(dve, qT_done, n - 1)
                for k in range(NBLK):
                    nc.vector.tensor_scalar(xn[u % 2][:, k, :], X[:, n, k, :], mv[u % 2][:, k, 0:1], rstd[u % 2][:, k:k + 1],
                                            ALU.subtract, ALU.mult).then_inc(xn_done, 1)

            dve.wait_ge(x_in[0], 16)
            stats1(0, 0)
            dve.wait_ge(consts_in, 16 * N_CONST_LOADS)
            nc.vector.memset(wg[:, :, 2 * NH:NG], 0.0).then_inc(wg_mean0, 1)
            dve.wait_ge(wg_mean0, 1)
            for c in range(NCH):
                for j in range(P // DH):
                    h = c * (P // DH) + j
                    nc.vector.memset(wg[j * DH:(j + 1) * DH, NCH + c, 2 * NH + h:2 * NH + h + 1], -1.0 / DH).then_inc(wg_ready, 1)
            for w, o in ((wi, 0), (wf, NH)):
                nc.vector.tensor_copy(wg[:, 0:NCH, o:o + NH], w[:, 0:NCH, :]).then_inc(wg_ready, 1)
                nc.vector.tensor_tensor(wg[:, NCH:2 * NCH, o:o + NH], w[:, NCH:2 * NCH, :], w[:, 2 * NCH:3 * NCH, :],
                                        ALU.add).then_inc(wg_ready, 1)
            dve.wait_ge(tanh_done, 1)
            nc.vector.tensor_scalar(scale_g[:], scale_in[:], tanh_g[:, 0:1], None, ALU.mult).then_inc(scale_done, 1)

            for n in range(1, SLOTS1):
                dve.wait_ge(x_in[n], 16)
                stats1(n, n)
                norm1(n - 1, n - 1)
            with dve.Fori(1, B // SLOTS1) as turn:
                for u in range(SLOTS1):
                    n = SLOTS1 * turn + u
                    dve.wait_ge(x_in[u], 16 * (turn + 1))
                    stats1(n, u)
                    norm1(n - 1, (u - 1) % SLOTS1)
            norm1(B - 1, SLOTS1 - 1)

            nc.vector.tensor_scalar(w_pos[:], w_in[:], 0.0, None, ALU.is_gt).then_inc(w_split, 1)
            nc.vector.tensor_scalar(w_neg[:], w_in[:], 0.0, None, ALU.is_lt).then_inc(w_split, 1)
            dve.wait_ge(w_split, 2)
            nc.vector.tensor_tensor(w_pos[:], w_pos[:], w_neg[:], ALU.subtract).then_inc(w_sign, 1)

            dve.wait_ge(gates_copied, B)

            def gate_cols(o):
                return G[:, :, :, o:o + NH].rearrange("p b k h -> p k b h")

            for dst, o, done in ((gf, NH, gf_done), (gi, 0, gi_done)):
                for k in range(NBLK):
                    nc.vector.tensor_tensor(dst[:, k, :].rearrange("p (b h) -> p b h", b=B), G[:, :, k, o:o + NH],
                                            gbias[:, o:o + NH].unsqueeze(1).to_broadcast([P, B, NH]), ALU.add).then_inc(done, 1)
            dve.wait_ge(gln_done, 1)
            nc.vector.scalar_tensor_tensor(logf[:], gf[:], 0.0, gln[:], ALU.min, ALU.subtract).then_inc(logf_done, 1)
            dve.wait_ge(frow_done, 2)
            dve.wait_ge(zeros_ready, 1)
            nc.vector.tensor_tensor_scan(cs[:], ps_frow, zeros[:], 0.0, ALU.add, ALU.add).then_inc(cs_done, 1)
            dve.wait_ge(irow_done, 2)
            dve.wait_ge(cs_done, 1)
            nc.vector.tensor_tensor(a_row[:], ps_irow, cs[:], ALU.subtract).then_inc(a_done, 1)
            dve.wait_ge(a_done, 1)
            nc.vector.tensor_tensor_scan(m_row[:], a_row[:], a_row[:], -3.0e38, ALU.max, ALU.max).then_inc(m_done, 1)
            dve.wait_ge(m_done, 1)
            nc.vector.tensor_tensor(maxd_row[:], cs[:], m_row[:], ALU.add).then_inc(maxd_done, 1)

            def decay(n, u, h):
                dve.wait_ge(qk_done, 4 * n + h + 1)
                dve.wait_ge(mask_done, 4 * n + h + 1)
                need(dve, num_done, n - 1)
                nc.vector.tensor_tensor(C[u][:, h, :], ps_qk[h % 2][:, 0:DW], D[u][:, h, :], ALU.mult).then_inc(c_done, 1)

            def head_sums(n, u):
                dve.wait_ge(sq_done, n + 1)
                need(dve, varn_done, n)
                nc.vector.tensor_reduce(ssq, sq, AX.X, ALU.add).then_inc(ssq_done, 1)
                need(dve, nb_done, n)
                sums = ps_num[u][:, :, :, DH]
                nc.vector.scalar_tensor_tensor(nrm_a[:].rearrange("p (k h) -> p k h", k=NBLK), sums, -1.0,
                                               floor_col[:, :, bass.ds(NH * n, NH)], ALU.mult, ALU.max).then_inc(na_done, 1)
                dve.wait_ge(na_done, n + 1)
                need(dve, nc_done, n)
                nc.vector.tensor_tensor(nrm_b[:].rearrange("p (k h) -> p k h", k=NBLK), sums,
                                        nrm_a[:].rearrange("p (k h) -> p k h", k=NBLK), ALU.max).then_inc(nb_done, 1)

            def head_norm(n, u):
                dve.wait_ge(hrs_done, n + 1)
                need(dve, hsc_done, n)
                nc.vector.tensor_tensor(hn.rearrange("p (k h) d -> p k h d", k=NBLK), ps_num[u][:, :, :, 0:DH],
                                        hrs[:].rearrange("p (k h) -> p k h", k=NBLK).unsqueeze(3).to_broadcast([P, NBLK, NH, DH]),
                                        ALU.mult).then_inc(hn_done, 1)

            def stats2(n, u):
                dve.wait_ge(x2_done, n + 1)
                ln_stats(X[:, n], u, stats2_done, mv2_done, n, (mv2_done, 2 * (n - 1)), (xn2_done, 2 * (n - 1)))

            def norm2(n, u):
                dve.wait_ge(rstd2_done, n + 1)
                need(dve, x2T_done, n - 1)
                for k in range(NBLK):
                    nc.vector.tensor_scalar(xn[u][:, k, :], X[:, n, k, :], mv[u][:, k, 0:1], rstd[u][:, k:k + 1],
                                            ALU.subtract, ALU.mult).then_inc(xn2_done, 1)

            def final(n):
                dve.wait_ge(ffn_done, n + 1)
                dve.wait_ge(x2_done, n + 1)
                nc.vector.scalar_tensor_tensor(X[:, n].rearrange("p k d -> p (k d)"), ps_f, tanh_g[:, 1:2],
                                               X[:, n].rearrange("p k d -> p (k d)"),
                                               ALU.mult, ALU.add).then_inc(out_done, 1)

            def step(n, u, first, last):
                live = range(first, last + 1)
                if 2 in live:
                    stats2(n - 2, u)
                if 0 in live:
                    decay(n, u, 0)
                    decay(n, u, 1)
                if 1 in live:
                    head_sums(n - 1, 1 - u)
                if 0 in live:
                    decay(n, u, 2)
                if 2 in live:
                    norm2(n - 2, u)
                if 0 in live:
                    decay(n, u, 3)
                if 1 in live:
                    head_norm(n - 1, 1 - u)
                if 3 in live:
                    final(n - 3)

            for n in range(0, 5):
                step(n, n % 2, 0, min(n, 3))
            with dve.Fori(2, (B - 2) // 2) as turn:
                for v in range(2):
                    step(2 * turn + 1 + v, (1 + v) % 2, 0, 3)
            for n in range(B - 1, LAST2):
                step(n, n % 2, n - B + 1, 3)

        @block.scalar
        def _(act):
            act.wait_ge(consts_in, 16 * N_CONST_LOADS)
            nc.scalar.activation(tanh_g[:], gates_in[:], ACT.Tanh).then_inc(tanh_done, 1)

            def copy_qkt(n, u, turn):
                need(act, qkt_saved[u], 16 * turn)
                act.wait_ge(cT_done, n + 1)
                nc.scalar.copy(qkt[u][:, 1].rearrange("p c s -> p (c s)"), ps_c[u % 2]).then_inc(cT_copied, 1)
                act.wait_ge(qT_done, n + 1)
                nc.scalar.copy(qkt[u][:, 0].rearrange("p c s -> p (c s)"), ps_q[u % 2]).then_inc(qT_copied, 1)

            def copy_gates(n, u):
                act.wait_ge(gates_done, n + 1)
                nc.scalar.copy(G[:, n], ps_g[u % 2]).then_inc(gates_copied, 1)

            for n in range(SLOTS1):
                copy_qkt(n, n, 0)
                if n:
                    copy_gates(n - 1, n - 1)
            with act.Fori(1, B // SLOTS1) as turn:
                for u in range(SLOTS1):
                    n = SLOTS1 * turn + u
                    copy_qkt(n, u, turn)
                    copy_gates(n - 1, (u - 1) % SLOTS1)
            copy_gates(B - 1, SLOTS1 - 1)

            act.wait_ge(gf_done, NBLK)
            nc.scalar.activation(gabs[:], gf[:], ACT.Abs).then_inc(gabs_done, 1)
            act.wait_ge(gabs_done, 1)
            nc.scalar.activation(gexp[:], gabs[:], ACT.Exp, scale=-1.0).then_inc(gexp_done, 1)
            act.wait_ge(gexp_done, 1)
            nc.scalar.activation(gln[:], gexp[:], ACT.Ln, bias=1.0).then_inc(gln_done, 1)
            act.wait_ge(w_turned, 4)
            nc.scalar.copy(sgnT[:].rearrange("p c o -> p (c o)"), ps_w).then_inc(w_copied, 1)
            act.wait_ge(cols_done, 4)
            nc.scalar.copy(a_col[:], ps_cols[:, 0]).then_inc(cols_copied, 1)
            nc.scalar.activation(floor_col[:], ps_cols[:, 1], ACT.Exp, bias=math.log(SCALE), scale=-1.0).then_inc(cols_copied, 1)
            act.wait_ge(cols_copied, 2)

            def decays(n, u, turn):
                act.wait_ge(m_in[u], 16 * (turn + 1))
                for h in range(NH):
                    need(act, c_done, 4 * (n - 2) + h + 1)
                    nc.scalar.activation(D[u][:, h, 0:S], m_all[u][:, h, :], ACT.Exp,
                                         bias=a_col[:, 0, bass.ds(NH * n + h, 1)], scale=-1.0)
                    nc.scalar.activation(D[u][:, h, S:DW], m_all[u][:, h, P:S], ACT.Exp,
                                         bias=a_col[:, 1, bass.ds(NH * n + h, 1)], scale=-1.0).then_inc(d_done, 1)

            def squares(n, u):
                act.wait_ge(num_done, n + 1)
                need(act, ssq_done, n)
                nc.scalar.activation(sq.rearrange("p (k h) d -> p k h d", k=NBLK), ps_num[u][:, :, :, 0:DH],
                                     ACT.Square).then_inc(sq_done, 1)

            def copy_x2T(n):
                act.wait_ge(x2T_done, n + 1)
                need(act, ffn_done, n)
                nc.scalar.copy(x2T.rearrange("p c s -> p (c s)"), ps_x).then_inc(x2T_copied, 1)

            def step(n, u, first, last, turn):
                live = range(first, last + 1)
                if 3 in live:
                    copy_x2T(n - 3)
                if 1 in live:
                    squares(n - 1, 1 - u)
                if -1 in live:
                    decays(n + 1, 1 - u, turn)

            decays(0, 0, 0)
            for n in range(0, 5):
                step(n, n % 2, -1, min(n, 3), (n + 1) // 2)
            with act.Fori(2, (B - 2) // 2) as turn:
                for v in range(2):
                    step(2 * turn + 1 + v, (1 + v) % 2, -1, 3, turn + 1)
            for n in range(B - 1, LAST2):
                step(n, n % 2, n - B + 1, 3, (n + 1) // 2)

        @block.tensor
        def _(pe):
            def turn_tile(dst, src, k_count, done):
                for c in range(NCH):
                    for k in range(k_count):
                        last = nc.tensor.transpose(dst[:, c * S + k * P:c * S + (k + 1) * P], src[:, k, c * P:(c + 1) * P], ident[:])
                last.then_inc(done, 1)

            pe.wait_ge(ident_ready, 1)
            pe.wait_ge(wg_ready, 2 * NCH + 4)

            def turn1(n, u):
                need(pe, cT_copied, n - 1)
                turn_tile(ps_c[u % 2], ctx_in[:, u], NBLK, cT_done)
                pe.wait_ge(xn_done, 2 * n + 2)
                need(pe, qT_copied, n - 1)
                turn_tile(ps_q[u % 2], xn[u % 2], NBLK, qT_done)

            def gates(n, u):
                pe.wait_ge(cT_copied, n + 1)
                pe.wait_ge(qT_copied, n + 1)
                need(pe, gates_copied, n - 1)
                for k in range(NBLK):
                    for c in range(2 * NCH):
                        last = nc.tensor.matmul(ps_g[u % 2][:, k, :], qkt[u][:, c // NCH, c % NCH, k * P:(k + 1) * P], wg[:, c, :],
                                                start=(c == 0), stop=(c == 2 * NCH - 1))
                last.then_inc(gates_done, 1)

            for n in range(SLOTS1):
                pe.wait_ge(c_in[n], 16)
                turn1(n, n)
                if n:
                    gates(n - 1, n - 1)
            with pe.Fori(1, B // SLOTS1) as turn:
                for u in range(SLOTS1):
                    n = SLOTS1 * turn + u
                    pe.wait_ge(c_in[u], 16 * (turn + 1))
                    turn1(n, u)
                    gates(n - 1, (u - 1) % SLOTS1)
            gates(B - 1, SLOTS1 - 1)

            pe.wait_ge(gi_done, NBLK)
            for k in range(NBLK):
                nc.tensor.transpose(ps_irow[:, k * P:(k + 1) * P], gi[:, k, :], ident[:]).then_inc(irow_done, 1)
            pe.wait_ge(logf_done, 1)
            for k in range(NBLK):
                nc.tensor.transpose(ps_frow[:, k * P:(k + 1) * P], logf[:, k, :], ident[:]).then_inc(frow_done, 1)
            pe.wait_ge(w_sign, 1)
            pe.wait_ge(qT_copied, B)
            for c in range(NCH):
                for k in range(NCH):
                    nc.tensor.transpose(ps_w[:, c * H + k * P:c * H + (k + 1) * P], w_pos[:, k, c * P:(c + 1) * P],
                                        ident[:]).then_inc(w_turned, 1)
            pe.wait_ge(a_done, 1)
            for k in range(NBLK):
                nc.tensor.transpose(ps_cols[:, 0, k, :], a_row[:, k * P:(k + 1) * P], ident[0:ROWS, 0:ROWS]).then_inc(cols_done, 1)
            pe.wait_ge(maxd_done, 1)
            for k in range(NBLK):
                nc.tensor.transpose(ps_cols[:, 1, k, :], maxd_row[:, k * P:(k + 1) * P], ident[0:ROWS, 0:ROWS]).then_inc(cols_done, 1)
            pe.wait_ge(gates_copied, B)
            pe.wait_ge(cols_copied, 2)
            pe.wait_ge(w_copied, 1)
            pe.wait_ge(v_done, B)

            def scores(n, u, h):
                need(pe, c_done, 4 * n + h - 1)
                r = slice((h % 2) * DH, (h % 2 + 1) * DH)
                nc.tensor.matmul(ps_qk[h % 2][:, 0:S], qkt[u][r, 1, h // 2, 0:P], qkt[u][r, 0, h // 2, 0:S], start=True, stop=True)
                nc.tensor.matmul(ps_qk[h % 2][:, S:DW], qkt[u][r, 1, h // 2, P:S], qkt[u][r, 0, h // 2, P:S],
                                 start=True, stop=True).then_inc(qk_done, 1)

            def values(n, u, h):
                pe.wait_ge(c_done, 4 * n + h + 1)
                nc.tensor.matmul(ps_num[u][:, 0, h, :], C[u][:, h, 0:P], V1[:, n, 0, h, :], start=True, stop=True)
                nc.tensor.matmul(ps_num[u][:, 1, h, :], C[u][:, h, P:S], V1[:, n, 0, h, :], start=True, stop=False)
                last = nc.tensor.matmul(ps_num[u][:, 1, h, :], C[u][:, h, S:DW], V1[:, n, 1, h, :], start=False, stop=True)
                if h == NH - 1:
                    last.then_inc(num_done, 1)

            def turn2(n, u):
                pe.wait_ge(xn2_done, 2 * n + 2)
                need(pe, x2T_copied, n)
                turn_tile(ps_x, xn[u], NBLK, x2T_done)

            def ffn(n):
                pe.wait_ge(x2T_copied, n + 1)
                need(pe, out_done, n)
                for k in range(NBLK):
                    for c in range(NCH):
                        last = nc.tensor.matmul(ps_f[:, k * H:(k + 1) * H], x2T[:, c, k * P:(k + 1) * P], sgnT[:, c, :],
                                                start=(c == 0), stop=(c == NCH - 1))
                last.then_inc(ffn_done, 1)

            def step(n, u, first, last, turn):
                live = range(first, last + 1)
                if 0 in live:
                    pe.wait_ge(qkt_in[u], 16 * (turn + 1))
                    scores(n, u, 0)
                    scores(n, u, 1)
                if 3 in live:
                    ffn(n - 3)
                if 0 in live:
                    scores(n, u, 2)
                    scores(n, u, 3)
                    need(pe, hn_done, n - 1)
                    for h in range(NH):
                        values(n, u, h)
                if 2 in live:
                    turn2(n - 2, u)

            for n in range(0, 5):
                step(n, n % 2, 0, min(n, 3), n // 2)
            with pe.Fori(2, (B - 2) // 2) as turn:
                step(2 * turn + 1, 1, 0, 3, turn)
                step(2 * turn + 2, 0, 0, 3, turn + 1)
            for n in range(B - 1, LAST2):
                step(n, n % 2, n - B + 1, 3, n // 2)


_INS = ["x", "ctx_1024", "g_xattn", "g_ffn", "L0_xattn_igate_kernel", "L0_xattn_igate_bias", "L0_xattn_fgate_kernel",
        "L0_xattn_fgate_bias", "L0_xattn_outnorm_scale", "L0_ffn_weight"]


def kernel(**inputs):
    import numpy as np
    import concourse.bacc as bacc
    from concourse.bass_utils import run_bass_kernel_spmd

    nc = bacc.Bacc("TRN2", target_bir_lowering=False, num_devices=1)
    arrays, args = {}, []
    for name in _INS:
        a = np.ascontiguousarray(inputs[name])
        arrays[f"in_{name}"] = a
        args.append(nc.dram_tensor(f"in_{name}", a.shape, mybir.dt.from_np(a.dtype), kind="ExternalInput").ap())
    x = inputs["x"]
    args.append(nc.dram_tensor("out", x.shape, mybir.dt.from_np(np.dtype("float32")), kind="ExternalOutput").ap())
    build(nc, *args)
    r = run_bass_kernel_spmd(nc, [arrays], core_ids=[0])
    return r.results[0]["out"]
```

```python
import math
from contextlib import ExitStack

import concourse.bass as bass
from concourse import mybir


def build(nc, x, ctx, g_xattn, g_ffn, igate_kernel, igate_bias, fgate_kernel, fgate_bias,
          outnorm_scale, ffn_weight, out):
    fp32 = mybir.dt.float32
    ALU = mybir.AluOpType
    ACT = mybir.ActivationFunctionType
    AX = mybir.AxisListType

    P = 128
    B, S, H = x.shape
    NH = igate_bias.shape[0]
    DH = H // NH
    NBLK = S // P
    NCH = H // P
    ROWS = B * NH
    VW = DH + 1
    NG = 3 * NH
    LN_EPS = 1e-5
    EPS = 1e-6
    SCALE = math.sqrt(DH)
    KAPPA = math.sqrt(LN_EPS)
    ZSHIFT = 12
    SLOTS1 = 4
    DW = S + P

    x_v = x.rearrange("b (k p) d -> b p k d", p=P)
    ctx_v = ctx.rearrange("b (k p) d -> b p k d", p=P)
    out_v = out.rearrange("b (k p) d -> b p k d", p=P)

    es = ExitStack()
    with es:
        def sb(name, shape, dt=fp32):
            return es.enter_context(nc.sbuf_tensor(name, shape, dt))

        def pb(name, shape):
            return es.enter_context(nc.psum_tensor(name, shape, fp32))

        def sem(name):
            return es.enter_context(nc.semaphore(name))

        X = sb("X", [P, B, NBLK, H])
        V1 = sb("V1", [P, B, NBLK, NH, VW])
        QKT = sb("QKT", [P, B, 2, NCH, S])
        qkt = [sb(f"qkt{u}", [P, 2, NCH, S]) for u in range(SLOTS1)]
        ctx_in = sb("ctx_in", [P, SLOTS1, NBLK, H])
        xn = [sb(f"xn{u}", [P, NBLK, H])[:] for u in range(2)]
        ident = sb("ident", [P, P])
        wi = sb("wi", [P, 3 * NCH, NH])
        wf = sb("wf", [P, 3 * NCH, NH])
        wg = sb("wg", [P, 2 * NCH, NG])
        gbias = sb("gbias", [P, 2 * NH])
        gates_in = sb("gates_in", [P, 2])
        tanh_g = sb("tanh_g", [P, 2])
        scale_in = sb("scale_in", [P, H])
        scale_g = sb("scale_g", [P, H])
        w_in = sb("w_in", [P, NCH, H])
        w_pos = sb("w_pos", [P, NCH, H])
        w_neg = sb("w_neg", [P, NCH, H])
        sgnT = sb("sgnT", [P, NCH, H])
        grow = [sb(f"grow{u}", [NG, S]) for u in range(2)]
        stats = [sb(f"stats{u}", [P, NBLK, 6]) for u in range(2)]
        mv = [sb(f"mv{u}", [P, NBLK, 2]) for u in range(2)]
        lnv = [sb(f"lnv{u}", [P, NBLK]) for u in range(2)]
        rough = [sb(f"rough{u}", [P, NBLK]) for u in range(2)]
        nwt_a = sb("nwt_a", [P, NBLK])
        nwt_b = sb("nwt_b", [P, NBLK])
        veps = [sb(f"veps{u}", [P, NBLK]) for u in range(2)]
        rstd = [sb(f"rstd{u}", [P, NBLK]) for u in range(2)]
        half_neg = sb("half_neg", [P, NBLK])
        G = sb("G", [P, B, NBLK, NG])
        gi = sb("gi", [P, NBLK, ROWS])
        gf = sb("gf", [P, NBLK, ROWS])
        gabs = sb("gabs", [P, NBLK, ROWS])
        gexp = sb("gexp", [P, NBLK, ROWS])
        gln = sb("gln", [P, NBLK, ROWS])
        logf = sb("logf", [P, NBLK, ROWS])
        zeros = sb("zeros", [ROWS, S])
        cs = sb("cs", [ROWS, S])
        a_row = sb("a_row", [ROWS, S])
        m_row = sb("m_row", [ROWS, S])
        maxd_row = sb("maxd_row", [ROWS, S])
        a_col = sb("a_col", [P, NBLK, ROWS])
        floor_col = sb("floor_col", [P, NBLK, ROWS])
        m_all = [qkt[2 + u][:].rearrange("p w c s -> p (w c) s") for u in range(2)]
        D = [sb(f"D{u}", [P, NH, DW]) for u in range(2)]
        C = [sb(f"C{u}", [P, NH, DW]) for u in range(2)]
        sq, hn, hsc = (ctx_in[:, i].rearrange("p k (h d) -> p (k h) d", d=DH) for i in range(3))
        x2T = ctx_in[:, 3]
        ssq = sb("ssq", [P, NBLK * NH])[:]
        nrm_a = sb("nrm_a", [P, NBLK * NH])
        nrm_b = sb("nrm_b", [P, NBLK * NH])
        nrm_c = sb("nrm_c", [P, NBLK * NH])
        nrm_d = sb("nrm_d", [P, NBLK * NH])
        zed = sb("zed", [P, NBLK * NH])
        zln = sb("zln", [P, NBLK * NH])
        zrough = sb("zrough", [P, NBLK * NH])
        nwt_c = sb("nwt_c", [P, NBLK * NH])
        nwt_d = sb("nwt_d", [P, NBLK * NH])
        hrs = sb("hrs", [P, NBLK * NH])
        m_dram = nc.dram_tensor("m_scratch", [ROWS, S], fp32, kind="Internal").ap()

        bank_n = [pb(f"bank_n{u}", [P, NBLK, 512]) for u in range(2)]
        bank_a = [pb(f"bank_a{u}", [P, 512]) for u in range(2)]
        bank_x = pb("bank_x", [P, 512])[:]
        bank_f = pb("bank_f", [P, 512])[:]
        ps_q = [bank_n[u][:, 0, :] for u in range(2)]
        ps_c = [bank_n[u][:, 1, :] for u in range(2)]
        ps_g = [bank_a[u][:, 0:NBLK * NG].rearrange("p (k g) -> p k g", k=NBLK) for u in range(2)]
        ps_r = [(bank_x, bank_f)[u][0:NG, 0:S] for u in range(2)]
        ps_irow = bank_x[0:ROWS, 0:S]
        ps_frow = bank_f[0:ROWS, 0:S]
        ps_cols = bank_n[0][:, 0, 0:2 * NBLK * ROWS].rearrange("p (w k r) -> p w k r", w=2, k=NBLK)
        ps_w = bank_n[1][:, 0, :]
        ps_num = [bank_n[u][:, :, 0:NH * VW].rearrange("p k (h v) -> p k h v", h=NH) for u in range(2)]
        ps_qk = bank_a
        ps_x = bank_x
        ps_f = bank_f

        consts_in = sem("consts_in")
        x_in = [sem(f"x_in{u}") for u in range(SLOTS1)]
        c_in = [sem(f"c_in{u}") for u in range(SLOTS1)]
        ident_zeroed, ident_ready, ones_ready, half_ready = sem("ident_zeroed"), sem("ident_ready"), sem("ones_ready"), sem("half_ready")
        zeros_ready = sem("zeros_ready")
        wg_mean0, wg_ready = sem("wg_mean0"), sem("wg_ready")
        tanh_done, scale_done = sem("tanh_done"), sem("scale_done")
        stats_done, mv_done, rstd_done, xn_done = sem("stats_done"), sem("mv_done"), sem("rstd_done"), sem("xn_done")
        lnv_done, rough_done, nwt_a_done, nwt_b_done = sem("lnv_done"), sem("rough_done"), sem("nwt_a_done"), sem("nwt_b_done")
        qT_saved = sem("qT_saved")
        qT_done, cT_done, qT_copied, cT_copied = sem("qT_done"), sem("cT_done"), sem("qT_copied"), sem("cT_copied")
        gates_done, gates_copied, v_done = sem("gates_done"), sem("gates_copied"), sem("v_done")
        rows_copied, gates_turned = sem("rows_copied"), sem("gates_turned")
        qkt_saved = [sem(f"qkt_saved{u}") for u in range(SLOTS1)]
        w_split, w_sign, w_turned, w_copied = sem("w_split"), sem("w_sign"), sem("w_turned"), sem("w_copied")
        gi_done, gf_done, gabs_done, gexp_done, gln_done, logf_done = (sem("gi_done"), sem("gf_done"), sem("gabs_done"),
                                                                     sem("gexp_done"), sem("gln_done"), sem("logf_done"))
        irow_done, frow_done, cs_done, a_done, m_done, maxd_done = (sem("irow_done"), sem("frow_done"), sem("cs_done"),
                                                                  sem("a_done"), sem("m_done"), sem("maxd_done"))
        cols_done, cols_copied, m_saved = sem("cols_done"), sem("cols_copied"), sem("m_saved")
        qkt_in = [sem(f"qkt_in{u}") for u in range(2)]
        m_in = [sem(f"m_in{u}") for u in range(2)]
        d_done, mask_done, qk_done, c_done, num_done = sem("d_done"), sem("mask_done"), sem("qk_done"), sem("c_done"), sem("num_done")
        sq_done, ssq_done, na_done, nb_done, nc_done, nd_done = (sem("sq_done"), sem("ssq_done"), sem("na_done"),
                                                               sem("nb_done"), sem("nc_done"), sem("nd_done"))
        zln_done, zrough_done, nwt_c_done, nwt_d_done = sem("zln_done"), sem("zrough_done"), sem("nwt_c_done"), sem("nwt_d_done")
        zed_done, hrs_done, hn_done, hsc_done, x2_done = (sem("zed_done"), sem("hrs_done"),
                                                                   sem("hn_done"), sem("hsc_done"), sem("x2_done"))
        stats2_done, mv2_done, veps2_done, rstd2_done, xn2_done = (sem("stats2_done"), sem("mv2_done"), sem("veps2_done"),
                                                                 sem("rstd2_done"), sem("xn2_done"))
        x2T_done, x2T_copied, ffn_done, out_done = sem("x2T_done"), sem("x2T_copied"), sem("ffn_done"), sem("out_done")
        stored = sem("stored")
        held = {e: sem(f"held_{e}") for e in ("SP", "Pool", "DVE", "PE")}
        N_CONST_LOADS = 8

        def need(eng, s, count):
            if not (isinstance(count, int) and count <= 0):
                eng.wait_ge(s, count)

        def hold(eng, s, count):
            if isinstance(count, int):
                need(eng, s, count)
            else:
                eng.wait_ge(s, count).then_inc(held[eng.engine.name], 1)

        block = es.enter_context(nc.Block())

        LAST2 = B + 4

        @block.sync
        def _(sp):
            def load_x(n, u, turn):
                if turn is not None:
                    hold(sp, x_in[u], 16 * turn)
                sp.dma_start(X[:, n], x_v[n]).then_inc(x_in[u], 16)

            def load_ctx(n, u, turn):
                if turn is not None:
                    hold(sp, c_in[u], 16 * turn)
                    hold(sp, v_done, n - 3)
                sp.dma_start(ctx_in[:, u], ctx_v[n]).then_inc(c_in[u], 16)

            def save_cT(n, u):
                hold(sp, cT_copied, n + 1)
                sp.dma_start(QKT[:, n, 1], qkt[u][:, 1]).then_inc(qkt_saved[u], 16)

            load_x(0, 0, None)
            sp.dma_start(wi[:], igate_kernel.rearrange("(c p) h -> p c h", p=P)).then_inc(consts_in, 16)
            sp.dma_start(wf[:], fgate_kernel.rearrange("(c p) h -> p c h", p=P)).then_inc(consts_in, 16)
            load_ctx(0, 0, None)
            sp.dma_start(gates_in[:, 0:1], g_xattn.partition_broadcast(P)).then_inc(consts_in, 16)
            sp.dma_start(gates_in[:, 1:2], g_ffn.partition_broadcast(P)).then_inc(consts_in, 16)
            load_x(1, 1, None)
            load_ctx(1, 1, None)
            sp.dma_start(scale_in[:], outnorm_scale.partition_broadcast(P)).then_inc(consts_in, 16)
            sp.dma_start(gbias[:, 0:NH], igate_bias.partition_broadcast(P)).then_inc(consts_in, 16)
            sp.dma_start(gbias[:, NH:2 * NH], fgate_bias.partition_broadcast(P)).then_inc(consts_in, 16)
            for n in range(2, SLOTS1):
                load_x(n, n, None)
                load_ctx(n, n, None)
            sp.dma_start(w_in[:], ffn_weight.rearrange("(c p) i -> p c i", p=P)).then_inc(consts_in, 16)
            for n in range(2):
                save_cT(n, n)
            with sp.Fori(1, B // SLOTS1) as turn:
                for u in range(SLOTS1):
                    load_x(SLOTS1 * turn + u, u, turn)
                    save_cT(SLOTS1 * turn + u - 2, (u - 2) % SLOTS1)
                    load_ctx(SLOTS1 * turn + u, u, turn)
            for n in range(B - 2, B):
                save_cT(n, n % SLOTS1)

            sp.wait_ge(m_done, 1)
            sp.dma_start(m_dram, m_row[:]).then_inc(m_saved, 16)
            sp.wait_ge(m_saved, 16)
            for u in range(SLOTS1):
                sp.wait_ge(qkt_saved[u], 16 * (B // 4))
            sp.wait_ge(gates_done, B)
            sp.wait_ge(qT_saved, B)

            def load2(n, u, turn):
                hold(sp, d_done, 4 * (n - 1))
                if not (isinstance(turn, int) and turn == 0):
                    hold(sp, m_in[u], 16 * turn)
                sp.dma_start(m_all[u], m_dram[bass.ds(NH * n, NH), :].rearrange("h s -> (h s)").partition_broadcast(P)
                             ).then_inc(m_in[u], 16)
                hold(sp, qk_done, 4 * (n - 1))
                if not (isinstance(turn, int) and turn == 0):
                    hold(sp, qkt_in[u], 16 * turn)
                sp.dma_start(qkt[u][:], QKT[:, n]).then_inc(qkt_in[u], 16)

            def store(n):
                hold(sp, out_done, n + 1)
                sp.dma_start(out_v[n], X[:, n]).then_inc(stored, 16)

            for n in range(6):
                load2(n, n % 2, n // 2)
            with sp.Fori(0, (B - 6) // 2) as turn:
                for u in range(2):
                    load2(2 * turn + 6 + u, u, turn + 3)
                    store(2 * turn + u)
            for n in range(B - 6, B):
                store(n)
            sp.wait_ge(stored, 16 * B)

        @block.gpsimd
        def _(pool):
            nc.gpsimd.memset(ident[:], 0.0).then_inc(ident_zeroed, 1)
            nc.gpsimd.memset(half_neg[:], -0.5).then_inc(half_ready, 1)
            nc.gpsimd.memset(V1[:, :, :, :, DH:VW].rearrange("p b k h o -> p (b k h) o"), 1.0).then_inc(ones_ready, 1)
            nc.gpsimd.memset(zeros[:], 0.0).then_inc(zeros_ready, 1)
            pool.wait_ge(ident_zeroed, 1)
            nc.gpsimd.affine_select(out=ident[:], in_=ident[:], compare_op=ALU.not_equal, fill=1.0, base=0,
                                    pattern=[[-1, P]], channel_multiplier=1).then_inc(ident_ready, 1)
            pool.wait_ge(half_ready, 1)

            def centre_v(n, u):
                pool.wait_ge(gates_copied, n + 1)
                mean = G[:, n, :, 2 * NH:NG]
                last = None
                for k in range(NBLK):
                    last = nc.gpsimd.tensor_tensor(
                        V1[:, n, k, :, 0:DH],
                        ctx_in[:, u, k, :].rearrange("p (h d) -> p h d", h=NH),
                        mean[:, k, :].unsqueeze(2).to_broadcast([P, NH, DH]), ALU.add)
                last.then_inc(v_done, 1)

            for n in range(1, SLOTS1):
                centre_v(n - 1, n - 1)
            with pool.Fori(1, B // SLOTS1) as turn:
                for u in range(SLOTS1):
                    centre_v(SLOTS1 * turn + u - 1, (u - 1) % SLOTS1)
            centre_v(B - 1, SLOTS1 - 1)

            def mask_head(n, u, h):
                hold(pool, d_done, 4 * n + h + 1)
                diag = D[u][:, h, :].rearrange("p (c s) -> p c s", s=P)[:, 0:3:2, :]
                nc.gpsimd.affine_select(out=diag, in_=diag, compare_op=ALU.is_ge, fill=0.0, base=0,
                                        pattern=[[0, 2], [1, P]], channel_multiplier=-1).then_inc(mask_done, 1)

            def floor_square(n):
                pool.wait_ge(nb_done, n + 1)
                hold(pool, zed_done, n)
                nc.gpsimd.tensor_scalar(nrm_c[:], nrm_b[:], SCALE * EPS * KAPPA, 2.0 ** 37, ALU.add, ALU.min).then_inc(nc_done, 1)
                pool.wait_ge(nc_done, n + 1)
                nc.gpsimd.tensor_tensor(nrm_d[:], nrm_c[:], nrm_c[:], ALU.mult).then_inc(nd_done, 1)

            def residual_scale(n):
                pool.wait_ge(hn_done, n + 1)
                need(pool, x2_done, n)
                nc.gpsimd.tensor_tensor(hsc.rearrange("p (k h) d -> p k (h d)", k=NBLK),
                                        hn.rearrange("p (k h) d -> p k (h d)", k=NBLK),
                                        scale_g[:].unsqueeze(1).to_broadcast([P, NBLK, H]), ALU.mult).then_inc(hsc_done, 1)

            def residual_add(n):
                pool.wait_ge(hsc_done, n + 1)
                nc.gpsimd.tensor_tensor(X[:, n], hsc.rearrange("p (k h) d -> p k (h d)", k=NBLK), X[:, n], ALU.add
                                        ).then_inc(x2_done, 1)

            def rsqrt2(n, u):
                pool.wait_ge(mv2_done, 2 * n + 2)
                hold(pool, rstd2_done, n - 1)
                nc.gpsimd.tensor_scalar(veps[u][:], mv[u][:, :, 1], LN_EPS, None, ALU.add).then_inc(veps2_done, 1)
                pool.wait_ge(veps2_done, n + 1)
                need(pool, xn2_done, 2 * (n - 1))
                nc.gpsimd.tensor_tensor(rstd[u][:], veps[u][:], half_neg[:], ALU.pow).then_inc(rstd2_done, 1)

            def step(n, u, first, last):
                live = range(first, last + 1)
                if 3 in live:
                    rsqrt2(n - 3, 1 - u)
                if 2 in live:
                    residual_scale(n - 2)
                if -1 in live:
                    mask_head(n + 1, 1 - u, 0)
                    mask_head(n + 1, 1 - u, 1)
                if 1 in live:
                    floor_square(n - 1)
                if 2 in live:
                    residual_add(n - 2)
                if -1 in live:
                    mask_head(n + 1, 1 - u, 2)
                    mask_head(n + 1, 1 - u, 3)

            pool.wait_ge(scale_done, 1)
            for h in range(NH):
                mask_head(0, 0, h)
            for n in range(0, 5):
                step(n, n % 2, -1, min(n, 4))
            with pool.Fori(2, (B - 2) // 2) as turn:
                for v in range(2):
                    step(2 * turn + 1 + v, (1 + v) % 2, -1, 4)
            for n in range(B - 1, LAST2):
                step(n, n % 2, n - B + 1, 4)

        @block.vector
        def _(dve):
            def stats1(n, u, before):
                u = u % 2
                need(dve, mv_done, 2 * (n - 1))
                newton = newton1(n - 1, 1 - u) if before else iter([None] * 3)
                nc.vector.bn_stats(stats[u][:, 0, :], X[:, n, 0, :]).then_inc(stats_done, 1)
                next(newton)
                nc.vector.bn_stats(stats[u][:, 1, :], X[:, n, 1, :]).then_inc(stats_done, 1)
                next(newton)
                need(dve, xn_done, 2 * (n - 1))
                for k in range(NBLK):
                    hold(dve, stats_done, 2 * n + 1 + k)
                    nc.vector.bn_aggr(mv[u][:, k, :], stats[u][:, k, :]).then_inc(mv_done, 1)
                next(newton)

            def newton1(n, u):
                dve.wait_ge(rough_done, n + 1)
                nc.vector.scalar_tensor_tensor(nwt_a[:], rough[u][:], -0.5, rough[u][:], ALU.mult, ALU.mult).then_inc(nwt_a_done, 1)
                yield
                dve.wait_ge(nwt_a_done, n + 1)
                nc.vector.scalar_tensor_tensor(nwt_b[:], mv[u][:, :, 1], LN_EPS, nwt_a[:], ALU.add, ALU.mult).then_inc(nwt_b_done, 1)
                yield
                dve.wait_ge(nwt_b_done, n + 1)
                nc.vector.scalar_tensor_tensor(rstd[u][:], nwt_b[:], 1.5, rough[u][:], ALU.add, ALU.mult).then_inc(rstd_done, 1)
                yield

            def norm1(n, u):
                u = u % 2
                dve.wait_ge(rstd_done, n + 1)
                need(dve, qT_done, n - 1)
                for k in range(NBLK):
                    nc.vector.tensor_scalar(xn[u][:, k, :], X[:, n, k, :], mv[u][:, k, 0:1], rstd[u][:, k:k + 1],
                                            ALU.subtract, ALU.mult).then_inc(xn_done, 1)

            dve.wait_ge(x_in[0], 16)
            stats1(0, 0, False)
            dve.wait_ge(consts_in, 16 * N_CONST_LOADS)
            nc.vector.memset(wg[:, :, 2 * NH:NG], 0.0).then_inc(wg_mean0, 1)
            dve.wait_ge(wg_mean0, 1)
            for c in range(NCH):
                for j in range(P // DH):
                    h = c * (P // DH) + j
                    nc.vector.memset(wg[j * DH:(j + 1) * DH, NCH + c, 2 * NH + h:2 * NH + h + 1], -1.0 / DH).then_inc(wg_ready, 1)
            for w, o in ((wi, 0), (wf, NH)):
                nc.vector.tensor_copy(wg[:, 0:NCH, o:o + NH], w[:, 0:NCH, :]).then_inc(wg_ready, 1)
                nc.vector.tensor_tensor(wg[:, NCH:2 * NCH, o:o + NH], w[:, NCH:2 * NCH, :], w[:, 2 * NCH:3 * NCH, :],
                                        ALU.add).then_inc(wg_ready, 1)
            dve.wait_ge(tanh_done, 1)
            nc.vector.tensor_scalar(scale_g[:], scale_in[:], tanh_g[:, 0:1], None, ALU.mult).then_inc(scale_done, 1)

            for n in range(1, SLOTS1):
                dve.wait_ge(x_in[n], 16)
                stats1(n, n, True)
                norm1(n - 1, n - 1)
            with dve.Fori(1, B // SLOTS1) as turn:
                for u in range(SLOTS1):
                    n = SLOTS1 * turn + u
                    dve.wait_ge(x_in[u], 16 * (turn + 1))
                    stats1(n, u, True)
                    norm1(n - 1, (u - 1) % SLOTS1)
            for _ in newton1(B - 1, 1):
                pass
            norm1(B - 1, SLOTS1 - 1)

            nc.vector.tensor_scalar(w_pos[:], w_in[:], 0.0, None, ALU.is_gt).then_inc(w_split, 1)
            nc.vector.tensor_scalar(w_neg[:], w_in[:], 0.0, None, ALU.is_lt).then_inc(w_split, 1)
            dve.wait_ge(w_split, 2)
            nc.vector.tensor_tensor(w_pos[:], w_pos[:], w_neg[:], ALU.subtract).then_inc(w_sign, 1)

            dve.wait_ge(gates_copied, B)

            def gate_cols(o):
                return G[:, :, :, o:o + NH].rearrange("p b k h -> p k b h")

            for dst, o, done in ((gf, NH, gf_done), (gi, 0, gi_done)):
                for k in range(NBLK):
                    nc.vector.tensor_tensor(dst[:, k, :].rearrange("p (b h) -> p b h", b=B), G[:, :, k, o:o + NH],
                                            gbias[:, o:o + NH].unsqueeze(1).to_broadcast([P, B, NH]), ALU.add).then_inc(done, 1)
            dve.wait_ge(gln_done, 1)
            nc.vector.scalar_tensor_tensor(logf[:], gf[:], 0.0, gln[:], ALU.min, ALU.subtract).then_inc(logf_done, 1)
            dve.wait_ge(frow_done, 2)
            dve.wait_ge(zeros_ready, 1)
            nc.vector.tensor_tensor_scan(cs[:], ps_frow, zeros[:], 0.0, ALU.add, ALU.add).then_inc(cs_done, 1)
            dve.wait_ge(irow_done, 2)
            dve.wait_ge(cs_done, 1)
            nc.vector.tensor_tensor(a_row[:], ps_irow, cs[:], ALU.subtract).then_inc(a_done, 1)
            dve.wait_ge(a_done, 1)
            nc.vector.tensor_tensor_scan(m_row[:], a_row[:], a_row[:], -3.0e38, ALU.max, ALU.max).then_inc(m_done, 1)
            dve.wait_ge(m_done, 1)
            nc.vector.tensor_tensor(maxd_row[:], cs[:], m_row[:], ALU.add).then_inc(maxd_done, 1)

            def decay(n, u, h):
                dve.wait_ge(qk_done, 4 * n + h + 1)
                dve.wait_ge(mask_done, 4 * n + h + 1)
                need(dve, num_done, n - 1)
                nc.vector.tensor_tensor(C[u][:, h, :], ps_qk[h % 2][:, 0:DW], D[u][:, h, :], ALU.mult).then_inc(c_done, 1)

            def head_reduce(n, u):
                dve.wait_ge(sq_done, n + 1)
                nc.vector.tensor_reduce(ssq, sq, AX.X, ALU.add).then_inc(ssq_done, 1)
                nc.vector.scalar_tensor_tensor(nrm_a[:].rearrange("p (k h) -> p k h", k=NBLK), ps_num[u][:, :, :, DH], -KAPPA,
                                               floor_col[:, :, bass.ds(NH * n, NH)], ALU.mult, ALU.max).then_inc(na_done, 1)

            def head_normaliser(n, u):
                dve.wait_ge(na_done, n + 1)
                need(dve, nc_done, n)
                nc.vector.scalar_tensor_tensor(nrm_b[:].rearrange("p (k h) -> p k h", k=NBLK), ps_num[u][:, :, :, DH], KAPPA,
                                               nrm_a[:].rearrange("p (k h) -> p k h", k=NBLK), ALU.mult, ALU.max).then_inc(nb_done, 1)

            def head_z(n):
                dve.wait_ge(nd_done, n + 1)
                dve.wait_ge(ssq_done, n + 1)
                nc.vector.scalar_tensor_tensor(zed[:], ssq, 1.0 / DH, nrm_d[:], ALU.mult, ALU.add).then_inc(zed_done, 1)

            def head_newton(n):
                dve.wait_ge(zrough_done, n + 1)
                nc.vector.scalar_tensor_tensor(nwt_c[:], zrough[:], -0.5, zrough[:], ALU.mult, ALU.mult).then_inc(nwt_c_done, 1)
                yield
                dve.wait_ge(nwt_c_done, n + 1)
                nc.vector.tensor_tensor(nwt_d[:], zed[:], nwt_c[:], ALU.mult).then_inc(nwt_d_done, 1)
                yield
                dve.wait_ge(nwt_d_done, n + 1)
                nc.vector.scalar_tensor_tensor(hrs[:], nwt_d[:], 1.5, zrough[:], ALU.add, ALU.mult).then_inc(hrs_done, 1)
                yield

            def head_norm(n, u):
                dve.wait_ge(hrs_done, n + 1)
                need(dve, hsc_done, n)
                nc.vector.tensor_tensor(hn.rearrange("p (k h) d -> p k h d", k=NBLK), ps_num[u][:, :, :, 0:DH],
                                        hrs[:].rearrange("p (k h) -> p k h", k=NBLK).unsqueeze(3).to_broadcast([P, NBLK, NH, DH]),
                                        ALU.mult).then_inc(hn_done, 1)

            def stats2(n, u):
                dve.wait_ge(x2_done, n + 1)
                need(dve, mv2_done, 2 * (n - 1))
                for k in range(NBLK):
                    nc.vector.bn_stats(stats[u][:, k, :], X[:, n, k, :]).then_inc(stats2_done, 1)

            def aggregate2(n, u, k):
                need(dve, xn2_done, 2 * (n - 1))
                hold(dve, stats2_done, 2 * n + 1 + k)
                nc.vector.bn_aggr(mv[u][:, k, :], stats[u][:, k, :]).then_inc(mv2_done, 1)

            def norm2(n, u):
                dve.wait_ge(rstd2_done, n + 1)
                need(dve, x2T_done, n - 1)
                for k in range(NBLK):
                    nc.vector.tensor_scalar(xn[u][:, k, :], X[:, n, k, :], mv[u][:, k, 0:1], rstd[u][:, k:k + 1],
                                            ALU.subtract, ALU.mult).then_inc(xn2_done, 1)

            def final(n):
                dve.wait_ge(ffn_done, n + 1)
                dve.wait_ge(x2_done, n + 1)
                nc.vector.scalar_tensor_tensor(X[:, n].rearrange("p k d -> p (k d)"), ps_f, tanh_g[:, 1:2],
                                               X[:, n].rearrange("p k d -> p (k d)"),
                                               ALU.mult, ALU.add).then_inc(out_done, 1)

            def step(n, u, first, last):
                live = range(first, last + 1)
                if 0 in live:
                    decay(n, u, 0)
                    decay(n, u, 1)
                if 1 in live:
                    head_reduce(n - 1, 1 - u)
                if 0 in live:
                    decay(n, u, 2)
                if 1 in live:
                    head_normaliser(n - 1, 1 - u)
                if 0 in live:
                    decay(n, u, 3)
                if 4 in live:
                    final(n - 4)
                if 1 in live:
                    head_z(n - 1)
                if 3 in live:
                    norm2(n - 3, 1 - u)
                if 2 in live:
                    stats2(n - 2, u)
                newton = head_newton(n - 1) if 1 in live else iter([None] * 3)
                next(newton)
                if 2 in live:
                    aggregate2(n - 2, u, 0)
                next(newton)
                if 2 in live:
                    aggregate2(n - 2, u, 1)
                next(newton)
                if 1 in live:
                    head_norm(n - 1, 1 - u)

            for n in range(0, 5):
                step(n, n % 2, 0, min(n, 4))
            with dve.Fori(2, (B - 2) // 2) as turn:
                for v in range(2):
                    step(2 * turn + 1 + v, (1 + v) % 2, 0, 4)
            for n in range(B - 1, LAST2):
                step(n, n % 2, n - B + 1, 4)

        @block.scalar
        def _(act):
            act.wait_ge(consts_in, 16 * N_CONST_LOADS)
            nc.scalar.activation(tanh_g[:], gates_in[:], ACT.Tanh).then_inc(tanh_done, 1)
            nc.scalar.preload_act_table_set("natural_log_exp_and_others")

            def copy_cT(n, u, turn):
                need(act, qkt_saved[u], 16 * turn)
                need(act, gates_done, n - 3)
                act.wait_ge(cT_done, n + 1)
                nc.scalar.copy(qkt[u][:, 1].rearrange("p c s -> p (c s)"), ps_c[u % 2]).then_inc(cT_copied, 1)

            def rough_rsqrt(n, u):
                act.wait_ge(mv_done, 2 * n + 2)
                need(act, rstd_done, n - 1)
                nc.scalar.activation(lnv[u % 2][:], mv[u % 2][:, :, 1], ACT.Ln, bias=LN_EPS).then_inc(lnv_done, 1)
                act.wait_ge(lnv_done, n + 1)
                nc.scalar.activation(rough[u % 2][:], lnv[u % 2][:], ACT.Exp, scale=-0.5).then_inc(rough_done, 1)

            def copy_qT(n, u):
                need(act, gates_done, n - 3)
                act.wait_ge(qT_done, n + 1)
                nc.scalar.copy(qkt[u][:, 0].rearrange("p c s -> p (c s)"), ps_q[u % 2]).then_inc(qT_copied, 1)

            def save_qT(n, u):
                nc.scalar.copy(QKT[:, n, 0].rearrange("p c s -> p (c s)"), ps_q[u % 2]).then_inc(qT_saved, 1)

            def copy_rows(n, u):
                act.wait_ge(gates_done, n + 1)
                need(act, gates_turned, n - 1)
                nc.scalar.copy(grow[u % 2][:], ps_r[u % 2]).then_inc(rows_copied, 1)

            def copy_gates(n, u):
                act.wait_ge(gates_turned, n + 1)
                nc.scalar.copy(G[:, n], ps_g[u % 2]).then_inc(gates_copied, 1)

            for n in range(SLOTS1):
                rough_rsqrt(n, n)
                if n:
                    copy_qT(n - 1, n - 1)
                copy_cT(n, n, 0)
                if n:
                    save_qT(n - 1, n - 1)
                    if n >= 2:
                        copy_gates(n - 2, n - 2)
                    copy_rows(n - 1, n - 1)
            with act.Fori(1, B // SLOTS1) as turn:
                for u in range(SLOTS1):
                    n = SLOTS1 * turn + u
                    rough_rsqrt(n, u)
                    copy_qT(n - 1, (u - 1) % SLOTS1)
                    copy_cT(n, u, turn)
                    save_qT(n - 1, (u - 1) % SLOTS1)
                    copy_gates(n - 2, (u - 2) % SLOTS1)
                    copy_rows(n - 1, (u - 1) % SLOTS1)
            copy_qT(B - 1, SLOTS1 - 1)
            save_qT(B - 1, SLOTS1 - 1)
            copy_gates(B - 2, SLOTS1 - 2)
            copy_rows(B - 1, SLOTS1 - 1)
            copy_gates(B - 1, SLOTS1 - 1)

            act.wait_ge(gf_done, NBLK)
            nc.scalar.activation(gabs[:], gf[:], ACT.Abs).then_inc(gabs_done, 1)
            act.wait_ge(gabs_done, 1)
            nc.scalar.activation(gexp[:], gabs[:], ACT.Exp, scale=-1.0).then_inc(gexp_done, 1)
            act.wait_ge(gexp_done, 1)
            nc.scalar.activation(gln[:], gexp[:], ACT.Ln, bias=1.0).then_inc(gln_done, 1)
            act.wait_ge(w_turned, 4)
            nc.scalar.copy(sgnT[:].rearrange("p c o -> p (c o)"), ps_w).then_inc(w_copied, 1)
            act.wait_ge(cols_done, 4)
            nc.scalar.copy(a_col[:], ps_cols[:, 0]).then_inc(cols_copied, 1)
            nc.scalar.activation(floor_col[:], ps_cols[:, 1], ACT.Exp, bias=math.log(SCALE * KAPPA), scale=-1.0).then_inc(cols_copied, 1)
            act.wait_ge(cols_copied, 2)

            def decay_head(n, u, h):
                need(act, c_done, 4 * (n - 2) + h + 1)
                nc.scalar.activation(D[u][:, h, 0:S], m_all[u][:, h, :], ACT.Exp,
                                     bias=a_col[:, 0, bass.ds(NH * n + h, 1)], scale=-1.0)
                nc.scalar.activation(D[u][:, h, S:DW], m_all[u][:, h, P:S], ACT.Exp,
                                     bias=a_col[:, 1, bass.ds(NH * n + h, 1)], scale=-1.0).then_inc(d_done, 1)

            def squares(n, u):
                act.wait_ge(num_done, n + 1)
                need(act, ssq_done, n)
                nc.scalar.activation(sq.rearrange("p (k h) d -> p k h d", k=NBLK), ps_num[u][:, :, :, 0:DH],
                                     ACT.Square).then_inc(sq_done, 1)

            def head_rough_rsqrt(n):
                act.wait_ge(zed_done, n + 1)
                need(act, hrs_done, n)
                nc.scalar.activation(zln[:], zed[:], ACT.Ln, scale=2.0 ** -ZSHIFT).then_inc(zln_done, 1)
                act.wait_ge(zln_done, n + 1)
                nc.scalar.activation(zrough[:], zln[:], ACT.Exp, bias=-0.5 * ZSHIFT * math.log(2.0), scale=-0.5
                                     ).then_inc(zrough_done, 1)

            def copy_x2T(n):
                act.wait_ge(x2T_done, n + 1)
                need(act, ffn_done, n)
                nc.scalar.copy(x2T.rearrange("p c s -> p (c s)"), ps_x).then_inc(x2T_copied, 1)

            def step(n, u, first, last, turn):
                live = range(first, last + 1)
                if 4 in live:
                    copy_x2T(n - 4)
                if 1 in live:
                    squares(n - 1, 1 - u)
                if -1 in live:
                    act.wait_ge(m_in[1 - u], 16 * (turn + 1))
                    decay_head(n + 1, 1 - u, 0)
                    decay_head(n + 1, 1 - u, 1)
                    decay_head(n + 1, 1 - u, 2)
                if 1 in live:
                    head_rough_rsqrt(n - 1)
                if -1 in live:
                    decay_head(n + 1, 1 - u, 3)

            act.wait_ge(m_in[0], 16)
            for h in range(NH):
                decay_head(0, 0, h)
            for n in range(0, 5):
                step(n, n % 2, -1, min(n, 4), (n + 1) // 2)
            with act.Fori(2, (B - 2) // 2) as turn:
                for v in range(2):
                    step(2 * turn + 1 + v, (1 + v) % 2, -1, 4, turn + 1)
            for n in range(B - 1, LAST2):
                step(n, n % 2, n - B + 1, 4, (n + 1) // 2)

        @block.tensor
        def _(pe):
            def turn_tile(dst, src, k_count, done):
                for c in range(NCH):
                    for k in range(k_count):
                        last = nc.tensor.transpose(dst[:, c * S + k * P:c * S + (k + 1) * P], src[:, k, c * P:(c + 1) * P], ident[:])
                last.then_inc(done, 1)

            pe.wait_ge(ident_ready, 1)
            pe.wait_ge(wg_ready, 2 * NCH + 4)

            def turn_ctx(n, u):
                need(pe, cT_copied, n - 1)
                turn_tile(ps_c[u % 2], ctx_in[:, u], NBLK, cT_done)

            def turn_x(n, u):
                pe.wait_ge(xn_done, 2 * n + 2)
                need(pe, qT_saved, n - 1)
                turn_tile(ps_q[u % 2], xn[u % 2], NBLK, qT_done)

            def gates(n, u):
                pe.wait_ge(cT_copied, n + 1)
                pe.wait_ge(qT_copied, n + 1)
                need(pe, rows_copied, n - 1)
                for c in range(2 * NCH):
                    last = nc.tensor.matmul(ps_r[u % 2], wg[:, c, :], qkt[u][:, c // NCH, c % NCH, :],
                                            start=(c == 0), stop=(c == 2 * NCH - 1))
                last.then_inc(gates_done, 1)

            def turn_gates(n, u):
                pe.wait_ge(rows_copied, n + 1)
                hold(pe, gates_copied, n - 1)
                for k in range(NBLK):
                    last = nc.tensor.transpose(ps_g[u % 2][:, k, :], grow[u % 2][:, k * P:(k + 1) * P], ident[0:NG, 0:NG])
                last.then_inc(gates_turned, 1)

            for n in range(SLOTS1):
                if n:
                    turn_x(n - 1, n - 1)
                pe.wait_ge(c_in[n], 16)
                turn_ctx(n, n)
                if n >= 2:
                    turn_gates(n - 2, n - 2)
                if n:
                    gates(n - 1, n - 1)
            with pe.Fori(1, B // SLOTS1) as turn:
                for u in range(SLOTS1):
                    n = SLOTS1 * turn + u
                    turn_x(n - 1, (u - 1) % SLOTS1)
                    pe.wait_ge(c_in[u], 16 * (turn + 1))
                    turn_ctx(n, u)
                    turn_gates(n - 2, (u - 2) % SLOTS1)
                    gates(n - 1, (u - 1) % SLOTS1)
            turn_x(B - 1, SLOTS1 - 1)
            turn_gates(B - 2, SLOTS1 - 2)
            gates(B - 1, SLOTS1 - 1)
            turn_gates(B - 1, SLOTS1 - 1)

            pe.wait_ge(gi_done, NBLK)
            for k in range(NBLK):
                nc.tensor.transpose(ps_irow[:, k * P:(k + 1) * P], gi[:, k, :], ident[:]).then_inc(irow_done, 1)
            pe.wait_ge(logf_done, 1)
            for k in range(NBLK):
                nc.tensor.transpose(ps_frow[:, k * P:(k + 1) * P], logf[:, k, :], ident[:]).then_inc(frow_done, 1)
            pe.wait_ge(w_sign, 1)
            pe.wait_ge(qT_saved, B)
            for c in range(NCH):
                for k in range(NCH):
                    nc.tensor.transpose(ps_w[:, c * H + k * P:c * H + (k + 1) * P], w_pos[:, k, c * P:(c + 1) * P],
                                        ident[:]).then_inc(w_turned, 1)
            pe.wait_ge(a_done, 1)
            for k in range(NBLK):
                nc.tensor.transpose(ps_cols[:, 0, k, :], a_row[:, k * P:(k + 1) * P], ident[0:ROWS, 0:ROWS]).then_inc(cols_done, 1)
            pe.wait_ge(maxd_done, 1)
            for k in range(NBLK):
                nc.tensor.transpose(ps_cols[:, 1, k, :], maxd_row[:, k * P:(k + 1) * P], ident[0:ROWS, 0:ROWS]).then_inc(cols_done, 1)
            pe.wait_ge(gates_copied, B)
            pe.wait_ge(cols_copied, 2)
            pe.wait_ge(w_copied, 1)
            pe.wait_ge(v_done, B)

            def scores(n, u, h):
                need(pe, c_done, 4 * n + h - 1)
                r = slice((h % 2) * DH, (h % 2 + 1) * DH)
                nc.tensor.matmul(ps_qk[h % 2][:, 0:S], qkt[u][r, 1, h // 2, 0:P], qkt[u][r, 0, h // 2, 0:S], start=True, stop=True)
                nc.tensor.matmul(ps_qk[h % 2][:, S:DW], qkt[u][r, 1, h // 2, P:S], qkt[u][r, 0, h // 2, P:S],
                                 start=True, stop=True).then_inc(qk_done, 1)

            def values(n, u, h):
                pe.wait_ge(c_done, 4 * n + h + 1)
                nc.tensor.matmul(ps_num[u][:, 0, h, :], C[u][:, h, 0:P], V1[:, n, 0, h, :], start=True, stop=True)
                nc.tensor.matmul(ps_num[u][:, 1, h, :], C[u][:, h, P:S], V1[:, n, 0, h, :], start=True, stop=False)
                last = nc.tensor.matmul(ps_num[u][:, 1, h, :], C[u][:, h, S:DW], V1[:, n, 1, h, :], start=False, stop=True)
                if h == NH - 1:
                    last.then_inc(num_done, 1)

            def turn2(n, u):
                pe.wait_ge(xn2_done, 2 * n + 2)
                need(pe, x2T_copied, n)
                turn_tile(ps_x, xn[u], NBLK, x2T_done)

            def ffn(n):
                pe.wait_ge(x2T_copied, n + 1)
                need(pe, out_done, n)
                for k in range(NBLK):
                    for c in range(NCH):
                        last = nc.tensor.matmul(ps_f[:, k * H:(k + 1) * H], x2T[:, c, k * P:(k + 1) * P], sgnT[:, c, :],
                                                start=(c == 0), stop=(c == NCH - 1))
                last.then_inc(ffn_done, 1)

            def step(n, u, first, last, turn):
                live = range(first, last + 1)
                if 0 in live:
                    pe.wait_ge(qkt_in[u], 16 * (turn + 1))
                    scores(n, u, 0)
                    scores(n, u, 1)
                if 4 in live:
                    ffn(n - 4)
                if 0 in live:
                    scores(n, u, 2)
                    scores(n, u, 3)
                    need(pe, hn_done, n - 1)
                    for h in range(NH):
                        values(n, u, h)
                if 3 in live:
                    turn2(n - 3, 1 - u)

            for n in range(0, 5):
                step(n, n % 2, 0, min(n, 4), n // 2)
            with pe.Fori(2, (B - 2) // 2) as turn:
                step(2 * turn + 1, 1, 0, 4, turn)
                step(2 * turn + 2, 0, 0, 4, turn + 1)
            for n in range(B - 1, LAST2):
                step(n, n % 2, n - B + 1, 4, n // 2)


_INS = ["x", "ctx_1024", "g_xattn", "g_ffn", "L0_xattn_igate_kernel", "L0_xattn_igate_bias", "L0_xattn_fgate_kernel",
        "L0_xattn_fgate_bias", "L0_xattn_outnorm_scale", "L0_ffn_weight"]


def kernel(**inputs):
    import numpy as np
    import concourse.bacc as bacc
    from concourse.bass_utils import run_bass_kernel_spmd

    nc = bacc.Bacc("TRN2", target_bir_lowering=False, num_devices=1)
    arrays, args = {}, []
    for name in _INS:
        a = np.ascontiguousarray(inputs[name])
        arrays[f"in_{name}"] = a
        args.append(nc.dram_tensor(f"in_{name}", a.shape, mybir.dt.from_np(a.dtype), kind="ExternalInput").ap())
    x = inputs["x"]
    args.append(nc.dram_tensor("out", x.shape, mybir.dt.from_np(np.dtype("float32")), kind="ExternalOutput").ap())
    build(nc, *args)
    r = run_bass_kernel_spmd(nc, [arrays], core_ids=[0])
    return r.results[0]["out"]
```
